# Optimizing a Trainium2 kernel written in Bass

```python
import numpy as np
import jax
import jax.numpy as jnp

def _softmax(x, axis=-1):
    return jax.nn.softmax(x, axis=axis)

def _gelu(x):
    return jax.nn.gelu(x, approximate=True)

def _silu(x):
    return jax.nn.silu(x)

def _sigmoid(x):
    return jax.nn.sigmoid(x)

def _layernorm(x, axis=-1, eps=1e-05):
    m = jnp.mean(x, axis=axis, keepdims=True)
    v = jnp.var(x, axis=axis, keepdims=True)
    return (x - m) / jnp.sqrt(v + eps)

def _scatter_add(tgt, idx, src, axis=0):
    return tgt.at[idx].add(src)

def _segment_sum(src, seg, n):
    return jax.ops.segment_sum(src, seg, n)
kernel_name = 'mk_gnn_resnorm_d1_gnn_r32_9ddcfd'

def setup_inputs(seed: int=0):
    np.random.seed(seed)
    _w = jnp.asarray

    def _rec_inputs():
        import jax
        import jax.numpy as jnp
        _gk = jax.random.key(seed)
        x = -0.000202 + 1 * jax.random.normal(jax.random.fold_in(_gk, 1), (3125, 128), jnp.float32)
        _s = jax.random.randint(jax.random.fold_in(_gk, 2), (25000,), 0, 3125, jnp.int32)
        _d = jax.random.randint(jax.random.fold_in(_gk, 3), (25000,), 0, 3125, jnp.int32)
        _loop = jnp.arange(3125, dtype=jnp.int32)
        src = jnp.concatenate([_s, _d, _loop])
        dst = jnp.concatenate([_d, _s, _loop])
        _o = jnp.argsort(dst, stable=True)
        src = src[_o]
        dst = dst[_o]
        return (x, src, dst)
    x, src, dst = _rec_inputs()

    def _L0_gnn_setup():
        import jax, jax.numpy as jnp
        import numpy as np
        N_NODES = 50000
        N_EDGES = 12500
        D = 128
        NUM_LAYERS = 3
        DELTA = 4.0
        BN_EPS = 1e-05
        LN_EPS = 1e-05
        STD_EPS = 1e-30
        N_AGG = 4
        N_SCAL = 3

        def _pna_layer(h, src, dst, Mw, Mb, Uw, Ub, bn_g, bn_b, mix_w, mix_b):
            N = h.shape[0]
            msg = jnp.concatenate([h[src], h[dst]], axis=-1) @ Mw.T + Mb
            deg = jax.ops.segment_sum(jnp.ones((msg.shape[0],), msg.dtype), dst, num_segments=N)
            s1 = jax.ops.segment_sum(msg, dst, num_segments=N)
            s2 = jax.ops.segment_sum(msg * msg, dst, num_segments=N)
            mx = jax.ops.segment_max(msg, dst, num_segments=N)
            mn = jax.ops.segment_min(msg, dst, num_segments=N)
            degc = deg[:, None]
            mean = s1 / degc
            var = jax.nn.relu(s2 / degc - mean * mean)
            std = jnp.sqrt(var + STD_EPS)
            agg = jnp.concatenate([mx, mn, std, var], axis=-1)
            logd = jnp.log(deg + 1.0)[:, None]
            h_neigh = jnp.concatenate([agg, agg * (logd / DELTA), agg * (DELTA / logd)], axis=-1)
            u = jnp.concatenate([h, h_neigh], axis=-1) @ Uw.T + Ub
            u = u * jnp.sqrt(1.0 / N)
            mu = jnp.mean(u, axis=0)
            v = jnp.mean((u - mu) ** 2, axis=0)
            u = (u - mu) / jnp.sqrt(v + BN_EPS) * bn_g + bn_b
            out = jax.nn.leaky_relu(u @ mix_w.T + mix_b, 0.01)
            return out + h
        key = jax.random.key(seed)
        ks = jax.random.split(key, 8)
        L = NUM_LAYERS
        s = 0.05
        feat = jax.random.normal(ks[0], (N_NODES, D), jnp.float32)
        src = jax.random.randint(ks[1], (N_EDGES,), 0, N_NODES, dtype=jnp.int32)
        dst = jax.random.randint(ks[2], (N_EDGES,), 0, N_NODES, dtype=jnp.int32)
        u_in = (N_AGG * N_SCAL + 1) * D
        Mw = jax.random.normal(ks[3], (L, D, 2 * D), jnp.float32) * s
        Mb = jnp.zeros((L, D), jnp.float32)
        Uw = jax.random.normal(ks[4], (L, D, u_in), jnp.float32) * s
        Ub = jnp.zeros((L, D), jnp.float32)
        bn_g = jnp.ones((L, D), jnp.float32)
        bn_b = jnp.zeros((L, D), jnp.float32)
        mix_w = jax.random.normal(ks[5], (L, D, D), jnp.float32) * s
        mix_b = jnp.zeros((L, D), jnp.float32)
        ln_g = jnp.ones((L, D), jnp.float32)
        ln_b = jnp.zeros((L, D), jnp.float32)
        return dict(feat=feat, src=src, dst=dst, Mw=Mw, Mb=Mb, Uw=Uw, Ub=Ub, bn_g=bn_g, bn_b=bn_b, mix_w=mix_w, mix_b=mix_b, ln_g=ln_g, ln_b=ln_b)
    _L0_gnn_all = _L0_gnn_setup()
    _L0_gnn_in = {k: v for k, v in _L0_gnn_all.items() if k in ('Mw', 'Mb', 'Uw', 'Ub', 'bn_g', 'bn_b', 'mix_w', 'mix_b', 'ln_g', 'ln_b')}
    del _L0_gnn_all
    return {'x': x, 'src': src, 'dst': dst, 'L0_gnn_Mw': _L0_gnn_in['Mw'], 'L0_gnn_Mb': _L0_gnn_in['Mb'], 'L0_gnn_Uw': _L0_gnn_in['Uw'], 'L0_gnn_Ub': _L0_gnn_in['Ub'], 'L0_gnn_bn_g': _L0_gnn_in['bn_g'], 'L0_gnn_bn_b': _L0_gnn_in['bn_b'], 'L0_gnn_mix_w': _L0_gnn_in['mix_w'], 'L0_gnn_mix_b': _L0_gnn_in['mix_b'], 'L0_gnn_ln_g': _L0_gnn_in['ln_g'], 'L0_gnn_ln_b': _L0_gnn_in['ln_b']}

def reference(x, src, dst, L0_gnn_Mw, L0_gnn_Mb, L0_gnn_Uw, L0_gnn_Ub, L0_gnn_bn_g, L0_gnn_bn_b, L0_gnn_mix_w, L0_gnn_mix_b, L0_gnn_ln_g, L0_gnn_ln_b):
    import jax
    import jax.numpy as jnp

    def _L0_gnn_ref(feat, src, dst, Mw, Mb, Uw, Ub, bn_g, bn_b, mix_w, mix_b, ln_g, ln_b):
        import jax, jax.numpy as jnp
        import numpy as np
        N_NODES = 50000
        N_EDGES = 12500
        D = 128
        NUM_LAYERS = 3
        DELTA = 4.0
        BN_EPS = 1e-05
        LN_EPS = 1e-05
        STD_EPS = 1e-30
        N_AGG = 4
        N_SCAL = 3

        def _pna_layer(h, src, dst, Mw, Mb, Uw, Ub, bn_g, bn_b, mix_w, mix_b):
            N = h.shape[0]
            msg = jnp.concatenate([h[src], h[dst]], axis=-1) @ Mw.T + Mb
            deg = jax.ops.segment_sum(jnp.ones((msg.shape[0],), msg.dtype), dst, num_segments=N)
            s1 = jax.ops.segment_sum(msg, dst, num_segments=N)
            s2 = jax.ops.segment_sum(msg * msg, dst, num_segments=N)
            mx = jax.ops.segment_max(msg, dst, num_segments=N)
            mn = jax.ops.segment_min(msg, dst, num_segments=N)
            degc = deg[:, None]
            mean = s1 / degc
            var = jax.nn.relu(s2 / degc - mean * mean)
            std = jnp.sqrt(var + STD_EPS)
            agg = jnp.concatenate([mx, mn, std, var], axis=-1)
            logd = jnp.log(deg + 1.0)[:, None]
            h_neigh = jnp.concatenate([agg, agg * (logd / DELTA), agg * (DELTA / logd)], axis=-1)
            u = jnp.concatenate([h, h_neigh], axis=-1) @ Uw.T + Ub
            u = u * jnp.sqrt(1.0 / N)
            mu = jnp.mean(u, axis=0)
            v = jnp.mean((u - mu) ** 2, axis=0)
            u = (u - mu) / jnp.sqrt(v + BN_EPS) * bn_g + bn_b
            out = jax.nn.leaky_relu(u @ mix_w.T + mix_b, 0.01)
            return out + h
        N = feat.shape[0]
        loops = jnp.arange(N, dtype=src.dtype)
        src_sl = jnp.concatenate([src, loops])
        dst_sl = jnp.concatenate([dst, loops])
        h = feat
        for l in range(NUM_LAYERS):
            h = _pna_layer(h, src_sl, dst_sl, Mw[l], Mb[l], Uw[l], Ub[l], bn_g[l], bn_b[l], mix_w[l], mix_b[l])
            mu = jnp.mean(h, axis=-1, keepdims=True)
            v = jnp.mean((h - mu) ** 2, axis=-1, keepdims=True)
            h = (h - mu) / jnp.sqrt(v + LN_EPS) * ln_g[l] + ln_b[l]
            h = jax.nn.elu(h)
        return h
    x = _layernorm(x + _L0_gnn_ref(x, src, dst, L0_gnn_Mw, L0_gnn_Mb, L0_gnn_Uw, L0_gnn_Ub, L0_gnn_bn_g, L0_gnn_bn_b, L0_gnn_mix_w, L0_gnn_mix_b, L0_gnn_ln_g, L0_gnn_ln_b), axis=-1)
    return x

_drawn_inputs = setup_inputs


def setup_inputs(seed=0):
    import zlib

    import numpy as np

    out = dict(_drawn_inputs(seed))
    spreads = {'L0_gnn_Mb': (0.0, 0.8),
     'L0_gnn_Ub': (0.0, 0.8),
     'L0_gnn_bn_g': (1.0, 0.2),
     'L0_gnn_bn_b': (0.0, 0.1),
     'L0_gnn_mix_b': (0.0, 0.1),
     'L0_gnn_ln_g': (1.0, 0.2),
     'L0_gnn_ln_b': (0.0, 0.1)}
    factors = {}
    for name, (base, spread) in spreads.items():
        noise = np.random.default_rng([zlib.crc32(name.encode()), seed]).standard_normal(out[name].shape)
        drawn = base * np.exp(spread * noise) if base else spread * noise
        out[name] = jnp.asarray(drawn.astype(out[name].dtype))
    for name, factor in factors.items():
        out[name] = (out[name] * factor).astype(out[name].dtype)
    return out
```

```python
import math

import concourse.bass as bass
from concourse import mybir
from contextlib import ExitStack

FP32 = mybir.dt.float32
BF16 = mybir.dt.bfloat16
I32 = mybir.dt.int32
ALU = mybir.AluOpType
ACT = mybir.ActivationFunctionType
AX = mybir.AxisListType

P = 128


class Signal:

    def __init__(self, sem, per_layer, before=0):
        self.sem, self.per_layer, self.before = sem, per_layer, before

    def at(self, layer, k):
        return layer * self.per_layer + (self.before + k)


class Chain:

    def __init__(self, eng, sem):
        self.eng, self.sem, self.n = eng, sem, 0

    def step(self, ins):
        ins.then_inc(self.sem, 1)
        self.n += 1

    def wait(self):
        self.eng.wait_ge(self.sem, self.n)

    def restart(self):
        if self.n:
            self.wait()
            self.eng.sem_clear(self.sem)
            self.n = 0


def slot_plan(n_nodes, n_edges, n_tiles):
    mean = (n_edges - n_nodes) / n_nodes
    tail, law, beyond = 1.0, math.exp(-mean), []
    for k in range(4 * int(mean) + 64):
        tail -= law
        beyond.append(n_nodes * max(tail, 0.0))
        law *= mean / (k + 1)
    plan = []
    for t in range(n_tiles):
        most = 0.05 if t == 0 else P * t
        plan.append(next(k for k, b in enumerate(beyond) if b <= most))
    return [max(k, 8) for k in plan]


def build(nc, x, src, dst, w_pqu, b_qu, w_u, w_mix, v_cols, out):
    N, D = x.shape
    L = w_mix.shape[0]
    E = src.shape[0]
    T = -(-N // P)
    NP = T * P
    LAST = N - (T - 1) * P
    EP, EC = 125, E // 125
    HC = 25
    HCH = EC // HC
    PLAN = slot_plan(N, E, T)
    KW = PLAN[0]
    STRIDE = 8
    WL = KW + STRIDE
    NW = -(-(E // STRIDE + 1) // 16) * 16
    SP_LEN = STRIDE * (NW - 1) + WL
    BINS = 64
    BB = BINS // 4
    GW = 4
    GROUPS = []
    for t in range(T):
        full, rest = divmod(PLAN[t], GW)
        k0 = 0
        for j, nk in enumerate([GW] + [rest] * (rest > 0) + [GW] * (full - 1)):
            GROUPS.append((t, j, k0, nk))
            k0 += nk
    NG = len(GROUPS)
    R = 8
    SQ = 4
    slot_before, slot_total = [], [0] * R
    for n, (_, _, _, nk) in enumerate(GROUPS):
        slot_total[n % R] += 16 * nk
        slot_before.append(slot_total[n % R])
    tile_groups = [[n for n, g in enumerate(GROUPS) if g[0] == t] for t in range(T)]
    CH = [(c, min(4, T - c)) for c in range(0, T, 4)]
    NC = len(CH)
    INV_N = 1.0 / N
    BN_EPS, LN_EPS, STD_EPS, SLOPE, DELTA = 1e-5, 1e-5, 1e-30, 0.01, 4.0

    ctx = ExitStack()
    with ctx:
        def sb(name, shape, dt=FP32):
            return ctx.enter_context(nc.sbuf_tensor(name, shape, dt))

        def sem(name):
            return ctx.enter_context(nc.semaphore(name))

        src_pad = nc.dram_tensor("src_pad", [SP_LEN], I32).ap()
        windows = nc.dram_tensor("windows", [NW, WL], I32).ap()
        info_dram = nc.dram_tensor("info_by_rank", [NP, 4], I32).ap()
        p_table = nc.dram_tensor("p_table", [NP, D], FP32).ap()

        ident = sb("ident", [P, P])
        ones_d = sb("ones_d", [P, P])
        ones_f = sb("ones_f", [P, P])
        before_f = sb("before_f", [P, P])
        ones_b = sb("ones_b", [P, P], BF16)
        before_b = sb("before_b", [P, P], BF16)
        slot_no = sb("slot_no", [P, T, KW])
        node_no = sb("node_no", [P, T], I32)
        plan_sb = sb("plan_sb", [P, T])
        zeros_i = sb("zeros_i", [1, SP_LEN - E], I32)
        eps_ln = sb("eps_ln", [P, 1])
        eps_std = sb("eps_std", [P, 1])
        two_c = sb("two_c", [P, 1])
        dst_i = sb("dst_i", [EP, EC], I32)
        digit_i = sb("digit_i", [EP, 2, EC], I32)
        digit_b = sb("digit_b", [EP, 2, EC], BF16)
        deg = sb("deg", [P, T])
        start = sb("start", [P, T])
        small = sb("small", [P, 6, T])
        key_b = sb("key_b", [P, T], BF16)
        rank_i = sb("rank_i", [P, T], I32)
        info = sb("info", [P, T, 4], I32)
        info_r = sb("info_r", [P, T, 4], I32)
        row_i = sb("row_i", [P, T], I32)
        node_i = sb("node_i", [P, T], I32)
        bits_i = sb("bits_i", [P, 3, T], I32)
        bits_f = sb("bits_f", [P, 3, T])
        index = sb("index", [P, T, KW], I32)
        node_f = sb("node_f", [P, T])
        deg_r = sb("deg_r", [P, T])
        g_r = sb("g_r", [P, T])
        self_w = sb("self_w", [P, T])
        rdeg = sb("rdeg", [P, T])
        amp = sb("amp", [P, T])
        att = sb("att", [P, T])
        x_r = sb("x_r", [P, T, D])
        hT = sb("hT", [P, NP])
        uT = sb("uT", [P, NP])
        pqu = sb("pqu", [P, T, 3, D])
        w_pqu_sb = sb("w_pqu_sb", [P, 3 * D])
        b_qu_sb = sb("b_qu_sb", [P, 2 * D])
        w_u_sb = sb("w_u_sb", [P, 4, 3 * D])
        w_mix_sb = sb("w_mix_sb", [P, D])
        v_sb = sb("v_sb", [P, 5])
        base = sb("base", [P, 3, T * D])
        flat = base[:, :, :].rearrange("p a f -> p (a f)")
        base_min, base_s1, base_s2 = (base[:, i, :].rearrange("p (t d) -> p t d", d=D) for i in range(3))
        carved = [0]

        def carve(n):
            at = carved[0]
            carved[0] += n
            assert carved[0] <= 3 * T * D
            return flat[:, at:at + n]

        place = carve(2 * BINS * T).rearrange("p (a f) -> p a f", a=2)
        win_f = carve(2 * T * WL).rearrange("p (a f) -> p a f", a=2)
        win_i = carve(T * WL).bitcast(I32).rearrange("p (t k) -> p t k", k=WL)
        digits = carve(P * HC // 2).bitcast(BF16).rearrange("p (j c) -> p j c", c=HC)
        hot_bin = carve(BINS * T // 2).bitcast(BF16).rearrange("p (b t) -> p b t", t=T)
        start_r = sb("start_r", [P, T])
        extra_t = sb("extra_t", [T, 1])
        extra_f = sb("extra_f", [1, 2 * T + 1])
        extra_i = sb("extra_i", [1, 2 * T + 1], I32)
        ex_k = sb("ex_k", [P, 1])
        ex_f = sb("ex_f", [P, 4])
        ex_arc = sb("ex_arc", [P, 1], I32)
        ex_src = sb("ex_src", [P, 1], I32)
        ex_node = sb("ex_node", [P, 1], I32)
        ex_p = sb("ex_p", [P, 3, D])
        G = sb("G", [P, R, GW * D])
        hots_b = G[0:EP, :, :].rearrange("p r f -> p (r f)").bitcast(BF16)
        n_lo = 2 * P * HC
        hot_lo = hots_b[:, 0:n_lo].rearrange("p (b j c) -> p b j c", b=2, c=HC)
        hot_hi = hots_b[:, n_lo:n_lo + 2 * T * HC].rearrange("p (b j c) -> p b j c", b=2, c=HC)
        sq = sb("sq", [P, SQ, GW * D])
        acc = sb("acc", [P, 2, GW * D])
        tmp = sb("tmp", [P, 6, D])
        agg = sb("agg", [P, 2, 4 * D])
        aggT = sb("aggT", [P, 2, 4 * D])
        u_sb = sb("u_sb", [P, 2, D])
        bstats = sb("bstats", [P, T, 6])
        mv = sb("mv", [P, 8])
        cb = sb("cb", [P, 2, 2, 4 * D])
        fstats = sb("fstats", [P, 4, 6])
        fmv = sb("fmv", [P, 2, 4, 2])
        fsd = sb("fsd", [P, 2, 4])
        y_sb = sb("y_sb", [P, 2, 4 * D])
        o_sb = sb("o_sb", [P, 2, 4 * D])

        ps = ctx.enter_context(nc.psum_tensor("ps", [P, 8, 512], FP32))

        s_const = sem("constants_set")
        s_dst = sem("dst_loaded")
        s_srcp = sem("src_padded")
        s_win = sem("windows_laid")
        s_digits = sem("digit_hots")
        s_hist = sem("digit_hots_used")
        s_cnt = sem("degrees_counted")
        s_deg = sem("degrees_copied")
        s_pre = sem("degree_prefixes")
        s_bins = sem("bin_hots")
        s_places = sem("bin_places")
        s_info = sem("ranks_known")
        s_infod = sem("info_scattered")
        s_infor = sem("info_by_rank_loaded")
        s_rows = sem("window_rows_known")
        s_xr = sem("x_gathered")
        s_wing = sem("windows_gathered")
        s_idx = sem("indices_ready")
        s_xT = sem("x_transposed")
        s_lnd = sem("log_degree")
        s_xrz = sem("x_pad_zeroed")
        s_wc = sem("pqu_weights_loaded")
        s_wa = sem("layer_weights_loaded")
        s_dch = sem("dve_step")
        s_turn = sem("pool_turns")

        s_gT = sem("arc_counts_turned")
        s_most = sem("extra_counts_known")
        s_mostT = sem("extra_counts_turned")
        s_extra = sem("extra_counts_ready")
        x_arc = sem("extra_arcs_named")
        x_src = sem("extra_sources_gathered")
        x_node = sem("extra_nodes_named")
        x_p = sem("extra_rows_gathered")
        s_xch = sem("dve_extra_step")

        gathered = [Signal(sem(f"gathered{i}"), slot_total[i]) for i in range(R)]
        dve_used = Signal(sem("groups_compared"), NG)
        squared = Signal(sem("groups_squared"), NG)
        pe_used = Signal(sem("groups_summed"), NG)
        sums_read = Signal(sem("sums_read"), T)
        var_ready = Signal(sem("variance_ready"), T)
        std_ready = Signal(sem("deviation_ready"), T)
        agg_turned = Signal(sem("aggregates_turned"), T)
        agg_copied = Signal(sem("aggregates_copied"), T)
        z_done = Signal(sem("update_products"), T)
        u_ready = Signal(sem("update_ready"), T)
        u_turned = Signal(sem("update_turned"), T)
        u_copied = Signal(sem("update_copied"), T)
        bn_var = Signal(sem("bn_variance"), 1)
        bn_sd = Signal(sem("bn_deviation"), 1)
        bn_ready = Signal(sem("bn_ready"), 1)
        uhat = Signal(sem("normalised"), NC)
        mixed = Signal(sem("mixed"), NC)
        biased = Signal(sem("mix_biased"), NC)
        resid = Signal(sem("residual_added"), NC)
        mean_ps = Signal(sem("ln_means"), NC)
        centred = Signal(sem("centred"), NC)
        csq = Signal(sem("centred_squared"), NC)
        var_ps = Signal(sem("ln_variances"), NC)
        ln_log = Signal(sem("ln_logs"), NC)
        ln_sd = Signal(sem("ln_inverse_deviations"), NC)
        scaled = Signal(sem("ln_scaled"), NC)
        affine = Signal(sem("ln_affine"), NC)
        negpart = Signal(sem("negative_part"), NC)
        expd = Signal(sem("exponential"), NC)
        h_ready = Signal(sem("h_ready"), NC, before=NC)
        pqu_ps = Signal(sem("pqu_products"), T, before=T)
        p_copied = Signal(sem("p_copied"), T, before=T)
        qu_copied = Signal(sem("qu_copied"), T, before=T)
        p_scattered = Signal(sem("p_scattered"), 16 * T, before=16 * T)
        f_turned = sem("final_turned")
        f_added = sem("final_added")
        f_var = sem("final_variance")
        f_sd = sem("final_deviation")
        f_done = sem("final_done")
        f_out = [sem(f"outputs_scattered{i}") for i in range(2)]

        def rows_out(c):
            return 16 * sum(CH[i][1] for i in range(c % 2, c + 1, 2))

        block = ctx.enter_context(nc.Block())

        def hot(t):
            return slice(t * P, (t + 1) * P)

        def cols(c):
            t0, nt = CH[c]
            return slice(t0 * P, (t0 + nt) * P)

        def over_bins(ap):
            return ap.rearrange("p (q f) -> p q f", q=4)

        @block.sync
        def _(sp):
            sp.dma_start(dst_i[:, :], dst.rearrange("(p c) -> p c", p=EP)).then_inc(s_dst, 16)
            sp.wait_ge(s_const, 1)
            sp.dma_start(src_pad[0:E].rearrange("(p c) -> p c", p=EP),
                         src.rearrange("(p c) -> p c", p=EP)).then_inc(s_srcp, 16)
            sp.dma_start(src_pad[E:SP_LEN].rearrange("(a c) -> a c", a=1), zeros_i[:, :]).then_inc(s_srcp, 16)
            sp.dma_start(w_pqu_sb[:, :], w_pqu[0]).then_inc(s_wc, 16)
            sp.dma_start(b_qu_sb[:, :], b_qu[0:1, :].to_broadcast([P, 2 * D])).then_inc(s_wc, 16)
            sp.wait_ge(s_srcp, 32)
            sp.dma_start(windows, bass.AP(tensor=src_pad.tensor, offset=0,
                                          ap=[[STRIDE, NW], [1, WL]])).then_inc(s_win, 16)
            sp.wait_ge(s_infod, 16 * T)
            sp.dma_start(info_r[:, :, :], info_dram.rearrange("(t p) f -> p t f", p=P)).then_inc(s_infor, 16)

            def weights(l, last):
                if isinstance(l, int) and l == 0:
                    pass
                sp.dma_start(w_u_sb[:, :, :], w_u[bass.ds(l, 1)].rearrange("a p k f -> (a p) k f")
                             if not isinstance(l, int) else w_u[l]).then_inc(s_wa, 16)
                sp.dma_start(w_mix_sb[:, :], w_mix[bass.ds(l, 1)].rearrange("a p f -> (a p) f")
                             if not isinstance(l, int) else w_mix[l]).then_inc(s_wa, 16)
                sp.dma_start(v_sb[:, :], v_cols[bass.ds(l, 1)].rearrange("a p f -> (a p) f")
                             if not isinstance(l, int) else v_cols[l]).then_inc(s_wa, 16)

            weights(0, False)
            with sp.Fori(0, L - 1) as l:
                sp.wait_ge(pqu_ps.sem, pqu_ps.at(l, 0))
                sp.wait_ge(qu_copied.sem, qu_copied.at(l, 0))
                sp.dma_start(w_pqu_sb[:, :], w_pqu[bass.ds(l + 1, 1)].rearrange("a p f -> (a p) f")).then_inc(s_wc, 16)
                sp.dma_start(b_qu_sb[:, :], b_qu[bass.ds(l + 1, 1), :].to_broadcast([P, 2 * D])).then_inc(s_wc, 16)
                sp.wait_ge(affine.sem, affine.at(l, NC))
                weights(l + 1, True)

        @block.gpsimd
        def _(pool):
            g = nc.gpsimd
            g.memset(zeros_i[:, :], 0).then_inc(s_const, 1)
            g.iota(digits[:, :, :], [[1, P], [0, HC]], base=0, channel_multiplier=0,
                   allow_small_or_imprecise_dtypes=True).then_inc(s_const, 1)
            g.memset(ones_b[:, :], 1.0)
            g.memset(ones_f[:, :], 1.0)
            g.memset(ones_d[:, :], 1.0 / D)
            g.memset(ident[:, :], 0.0)
            g.memset(eps_ln[:, :], LN_EPS)
            g.memset(eps_std[:, :], STD_EPS)
            g.memset(two_c[:, :], 2.0)
            for t in range(T):
                g.memset(plan_sb[:, t:t + 1], float(PLAN[t]))
            g.memset(x_r[:, T - 1, :], 0.0)
            g.iota(slot_no[:, :, :], [[0, T], [1, KW]], base=0, channel_multiplier=0,
                   allow_small_or_imprecise_dtypes=True)
            g.iota(node_no[:, :], [[P, T]], base=0, channel_multiplier=1).then_inc(s_const, 1)
            pool.wait_ge(s_const, 3)
            g.affine_select(out=ident[:, :], in_=ident[:, :], compare_op=ALU.not_equal, fill=1.0,
                            base=0, pattern=[[-1, P]], channel_multiplier=1)
            g.affine_select(out=before_f[:, :], in_=ones_f[:, :], compare_op=ALU.is_gt, fill=0.0,
                            base=0, pattern=[[1, P]], channel_multiplier=-1)
            g.affine_select(out=before_b[:, :], in_=ones_b[:, :], compare_op=ALU.is_gt, fill=0.0,
                            base=0, pattern=[[1, P]], channel_multiplier=-1).then_inc(s_const, 1)
            pool.wait_ge(s_info, 1)
            for t in range(T):
                g.indirect_dma_start(info_dram, bass.IndirectOffsetOnAxis(ap=rank_i[:, t:t + 1], axis=0),
                                     info[:, t, :], None, bounds_check=NP - 1,
                                     oob_is_err=False).then_inc(s_infod, 16)
            pool.wait_ge(s_rows, 1)
            for t in range(T):
                g.indirect_dma_start(x_r[:, t, :], None, x,
                                     bass.IndirectOffsetOnAxis(ap=node_i[:, t:t + 1], axis=0),
                                     bounds_check=N - 1, oob_is_err=False).then_inc(s_xr, 16)
            pool.wait_ge(s_win, 16)
            for t in range(T):
                g.indirect_dma_start(win_i[:, t, :], None, windows,
                                     bass.IndirectOffsetOnAxis(ap=row_i[:, t:t + 1], axis=0),
                                     bounds_check=NW - 1, oob_is_err=False).then_inc(s_wing, 16)

            def scatter_p(l):
                for t in range(T):
                    pool.wait_ge(p_copied.sem, p_copied.at(l, t + 1))
                    pool.sem_inc(s_turn, 1)
                    g.indirect_dma_start(p_table, bass.IndirectOffsetOnAxis(ap=node_i[:, t:t + 1], axis=0),
                                         pqu[:, t, 0, :], None, bounds_check=NP - 1,
                                         oob_is_err=False).then_inc(p_scattered.sem, 16)

            def extras():
                with pool.If(pool.value_load(extra_i[0:1, T:T + 1], min_val=0, max_val=T * E) > 0):
                    with pool.Fori(0, T) as t:
                        more = pool.value_load(extra_i[0:1, bass.ds(t, 1)], min_val=0, max_val=T * E)
                        with pool.If(more > 0):
                            with pool.Fori(0, more):
                                pool.wait_ge(x_arc, 1)
                                pool.sem_clear(x_arc)
                                g.indirect_dma_start(ex_src[:, :], None,
                                                     src_pad.rearrange("(e a) -> e a", a=1),
                                                     bass.IndirectOffsetOnAxis(ap=ex_arc[:, :], axis=0))\
                                    .then_inc(x_src, 16)
                                pool.wait_ge(x_node, 1)
                                pool.sem_clear(x_node)
                                g.indirect_dma_start(ex_p[:, 0, :], None, p_table,
                                                     bass.IndirectOffsetOnAxis(ap=ex_node[:, :], axis=0))\
                                    .then_inc(x_p, 16)
                        pool.nop()
                    pool.nop()
                pool.nop()

            def gather(l):
                pool.wait_ge(p_scattered.sem, p_scattered.at(l, 0))
                pool.sem_inc(s_turn, 1)
                extras()
                for n, (t, _, k0, nk) in enumerate(GROUPS):
                    if n >= R:
                        pool.wait_ge(dve_used.sem, dve_used.at(l, n - R + 1))
                        pool.wait_ge(pe_used.sem, pe_used.at(l, n - R + 1))
                        pool.sem_inc(s_turn, 1)
                    for j in range(nk):
                        g.indirect_dma_start(G[:, n % R, j * D:(j + 1) * D], None, p_table,
                                             bass.IndirectOffsetOnAxis(ap=index[:, t, k0 + j:k0 + j + 1], axis=0))\
                            .then_inc(gathered[n % R].sem, 16)

            scatter_p(-1)
            pool.wait_ge(s_idx, 1)
            pool.wait_ge(s_extra, 1)
            with pool.Fori(0, L - 1) as l:
                gather(l)
                scatter_p(l)
            gather(L - 1)
            for t in range(T):
                pool.wait_ge(f_done, t + 1)
                g.indirect_dma_start(out, bass.IndirectOffsetOnAxis(ap=node_i[:, t:t + 1], axis=0),
                                     o_sb[:, (t // 4) % 2, (t % 4) * D:(t % 4 + 1) * D], None,
                                     bounds_check=N - 1, oob_is_err=False).then_inc(f_out[(t // 4) % 2], 16)
            for c in (NC - 2, NC - 1):
                pool.wait_ge(f_out[c % 2], rows_out(c))

        @block.tensor
        def _(pe):
            mm = nc.tensor.matmul
            cnt = ps[:, 0, 0:T]

            def count(b, first, last):
                for c in range(HC):
                    ins = mm(cnt, hot_lo[:, b, :, c], hot_hi[:, b, :, c],
                             start=first and c == 0, stop=last and c == HC - 1)
                return ins

            pe.wait_ge(s_digits, 1)
            count(0, True, False).then_inc(s_hist, 1)
            with pe.Fori(0, (HCH - 1) // 2 - 1) as i:
                pe.wait_ge(s_digits, 2 * i + 2)
                count(1, False, False).then_inc(s_hist, 1)
                pe.wait_ge(s_digits, 2 * i + 3)
                count(0, False, False).then_inc(s_hist, 1)
            pe.wait_ge(s_digits, HCH - 1)
            count(1, False, False).then_inc(s_hist, 1)
            pe.wait_ge(s_digits, HCH)
            count(0, False, True).then_inc(s_hist, 1)
            pe.wait_ge(s_const, 4)
            pe.wait_ge(s_deg, 1)
            mm(ps[:, 1, 0:T], before_f[:, :], deg[:, :], start=True, stop=True)
            mm(ps[:, 1, 32:32 + T], ones_f[:, :], deg[:, :], start=True, stop=True).then_inc(s_pre, 1)
            pe.wait_ge(s_bins, 1)
            hb = hot_bin[:, :, :].rearrange("p (q b) t -> p q (b t)", q=4)
            for q in range(4):
                mm(ps[:, q, 0:BB * T], before_b[:, :], hb[:, q, :], start=True, stop=True)
                ins = mm(ps[:, 4 + q, 0:BB * T], ones_b[:, :], hb[:, q, :], start=True, stop=True)
            ins.then_inc(s_places, 1)
            for c, (t0, nt) in enumerate(CH):
                if c == 0:
                    pe.wait_ge(s_xr, 16 * T)
                if c >= 2:
                    pe.wait_ge(h_ready.sem, c - 1)
                for i in range(nt):
                    ins = nc.tensor.transpose(ps[:, c % 2, i * D:(i + 1) * D], x_r[:, t0 + i, :], ident[:, :])
                ins.then_inc(s_xT, 1)

            def project(l, t):
                if t == 0:
                    pe.wait_ge(s_wc, 32 * (l + 2))
                if t % 4 == 0:
                    pe.wait_ge(h_ready.sem, h_ready.at(l, t // 4 + 1))
                if t >= 2:
                    pe.wait_ge(p_copied.sem, p_copied.at(l, t - 1))
                    pe.wait_ge(qu_copied.sem, qu_copied.at(l, t - 1))
                mm(ps[:, 4 + t % 2, 0:D], hT[:, hot(t)], w_pqu_sb[:, 0:D], start=True, stop=True)
                mm(ps[:, 6 + t % 2, 0:2 * D], hT[:, hot(t)], w_pqu_sb[:, D:3 * D],
                   start=True, stop=True).then_inc(pqu_ps.sem, 1)

            for t in range(T):
                project(-1, t)

            pe.wait_ge(s_idx, 1)
            nc.tensor.transpose(ps[0:T, 4, 0:P], small[:, 3, :], ident[:, :]).then_inc(s_gT, 1)
            pe.wait_ge(s_most, 1)
            nc.tensor.transpose(ps[0:1, 5, 0:T], extra_t[:, :], ident[0:T, 0:T]).then_inc(s_mostT, 1)

            def stage_a(l):
                for s in range(T + 3):
                    if s < T:
                        for n in tile_groups[s]:
                            _, j, _, nk = GROUPS[n]
                            w = nk * D
                            last = n == tile_groups[s][-1]
                            if j == 0 and s >= 2:
                                pe.wait_ge(sums_read.sem, sums_read.at(l, s - 1))
                            pe.wait_ge(gathered[n % R].sem, gathered[n % R].at(l, slot_before[n]))
                            mm(ps[:, s % 2, 0:w], ident[:, :], G[:, n % R, 0:w], start=j == 0, stop=last)
                            pe.wait_ge(squared.sem, squared.at(l, n + 1))
                            mm(ps[:, 2 + s % 2, 0:w], ident[:, :], sq[:, n % SQ, 0:w], start=j == 0,
                               stop=last).then_inc(pe_used.sem, 1)
                    t = s - 1
                    if 0 <= t < T:
                        pe.wait_ge(std_ready.sem, std_ready.at(l, t + 1))
                        if t >= 2:
                            pe.wait_ge(agg_copied.sem, agg_copied.at(l, t - 1))
                        for i in range(4):
                            ins = nc.tensor.transpose(ps[:, 4 + t % 2, i * D:(i + 1) * D],
                                                      agg[:, t % 2, i * D:(i + 1) * D], ident[:, :])
                        ins.then_inc(agg_turned.sem, 1)
                    t = s - 2
                    if 0 <= t < T:
                        if t == 0:
                            pe.wait_ge(s_wa, 48 * (l + 1))
                        pe.wait_ge(agg_copied.sem, agg_copied.at(l, t + 1))
                        if t >= 1:
                            pe.wait_ge(u_ready.sem, u_ready.at(l, t))
                        for i in range(4):
                            ins = mm(ps[:, 6, 0:3 * D], aggT[:, t % 2, i * D:(i + 1) * D], w_u_sb[:, i, :],
                                     start=i == 0, stop=i == 3)
                        ins.then_inc(z_done.sem, 1)
                    t = s - 3
                    if 0 <= t < T:
                        pe.wait_ge(u_ready.sem, u_ready.at(l, t + 1))
                        if t >= 1:
                            pe.wait_ge(u_copied.sem, u_copied.at(l, t))
                        nc.tensor.transpose(ps[:, 7, 0:D], u_sb[:, t % 2, :], ident[:, :])\
                            .then_inc(u_turned.sem, 1)

            def stage_b(l):
                for s in range(NC + 2):
                    c = s
                    if c < NC:
                        w = CH[c][1] * D
                        pe.wait_ge(uhat.sem, uhat.at(l, c + 1))
                        if c >= 2:
                            pe.wait_ge(biased.sem, biased.at(l, c - 1))
                        mm(ps[:, c % 2, 0:w], w_mix_sb[:, :], uT[:, cols(c)], start=True,
                           stop=True).then_inc(mixed.sem, 1)
                    c = s - 1
                    if 0 <= c < NC:
                        w = CH[c][1] * D
                        pe.wait_ge(resid.sem, resid.at(l, c + 1))
                        if c >= 2:
                            pe.wait_ge(centred.sem, centred.at(l, c - 1))
                        mm(ps[:, 2 + c % 2, 0:w], ones_d[:, :], hT[:, cols(c)], start=True,
                           stop=True).then_inc(mean_ps.sem, 1)
                    c = s - 2
                    if 0 <= c < NC:
                        w = CH[c][1] * D
                        pe.wait_ge(csq.sem, csq.at(l, c + 1))
                        if c >= 2:
                            pe.wait_ge(ln_sd.sem, ln_sd.at(l, c - 1))
                        mm(ps[:, 4 + c % 2, 0:w], ones_d[:, :], cb[:, 1, c % 2, 0:w], start=True,
                           stop=True).then_inc(var_ps.sem, 1)

            with pe.Fori(0, L - 1) as l:
                stage_a(l)
                stage_b(l)
                for t in range(T):
                    project(l, t)
            stage_a(L - 1)
            stage_b(L - 1)
            for c, (t0, nt) in enumerate(CH):
                pe.wait_ge(h_ready.sem, h_ready.at(L - 1, c + 1))
                if c >= 2:
                    pe.wait_ge(f_added, c - 1)
                for i in range(nt):
                    ins = nc.tensor.transpose(ps[:, 6 + c % 2, i * D:(i + 1) * D], hT[:, hot(t0 + i)], ident[:, :])
                ins.then_inc(f_turned, 1)

        @block.scalar
        def _(act):
            f = nc.scalar.activation
            for c in range(NC):
                act.wait_ge(s_xT, c + 1)
                f(hT[:, cols(c)], ps[:, c % 2, 0:CH[c][1] * D], ACT.Copy).then_inc(h_ready.sem, 1)

            def project(l, t):
                act.wait_ge(pqu_ps.sem, pqu_ps.at(l, t + 1))
                f(pqu[:, t, 0, :], ps[:, 4 + t % 2, 0:D], ACT.Copy).then_inc(p_copied.sem, 1)

            for t in range(T):
                project(-1, t)
            act.wait_ge(s_rows, 2)
            act.wait_ge(s_const, 3)
            f(amp[:, :], deg_r[:, :], ACT.Ln, bias=two_c[:, 0:1]).then_inc(s_lnd, 1)

            def stage_a(l):
                for s in range(T + 3):
                    if s < T:
                        for n in tile_groups[s]:
                            w = GROUPS[n][3] * D
                            act.wait_ge(gathered[n % R].sem, gathered[n % R].at(l, slot_before[n]))
                            if n >= SQ:
                                act.wait_ge(pe_used.sem, pe_used.at(l, n - SQ + 1))
                            f(sq[:, n % SQ, 0:w], G[:, n % R, 0:w], ACT.Square).then_inc(squared.sem, 1)
                        act.wait_ge(var_ready.sem, var_ready.at(l, s + 1))
                        f(agg[:, s % 2, 2 * D:3 * D], agg[:, s % 2, 3 * D:4 * D], ACT.Sqrt,
                          bias=eps_std[:, 0:1]).then_inc(std_ready.sem, 1)
                    t = s - 1
                    if 0 <= t < T:
                        act.wait_ge(agg_turned.sem, agg_turned.at(l, t + 1))
                        if t >= 2:
                            act.wait_ge(z_done.sem, z_done.at(l, t - 1))
                        f(aggT[:, t % 2, :], ps[:, 4 + t % 2, :], ACT.Copy).then_inc(agg_copied.sem, 1)
                    t = s - 3
                    if 0 <= t < T:
                        act.wait_ge(u_turned.sem, u_turned.at(l, t + 1))
                        f(uT[:, hot(t)], ps[:, 7, 0:D], ACT.Copy).then_inc(u_copied.sem, 1)
                act.wait_ge(bn_var.sem, bn_var.at(l, 1))
                f(mv[:, 3:4], mv[:, 2:3], ACT.Sqrt).then_inc(bn_sd.sem, 1)

            def stage_b(l, next_layer):
                nc.scalar.preload_act_table_set("natural_log_exp_and_others")
                act.wait_ge(bn_ready.sem, bn_ready.at(l, 1))
                for s in range(NC + 2):
                    c = s
                    if c < NC:
                        w = CH[c][1] * D
                        f(uT[:, cols(c)], uT[:, cols(c)], ACT.Identity, scale=mv[:, 4:5],
                          bias=mv[:, 6:7]).then_inc(uhat.sem, 1)
                        act.wait_ge(mixed.sem, mixed.at(l, c + 1))
                        if c >= 2:
                            act.wait_ge(resid.sem, resid.at(l, c - 1))
                        f(cb[:, 0, c % 2, 0:w], ps[:, c % 2, 0:w], ACT.Identity,
                          bias=v_sb[:, 2:3]).then_inc(biased.sem, 1)
                    c = s - 1
                    if 0 <= c < NC:
                        w = CH[c][1] * D
                        act.wait_ge(centred.sem, centred.at(l, c + 1))
                        if c >= 2:
                            act.wait_ge(scaled.sem, scaled.at(l, c - 1))
                        f(cb[:, 1, c % 2, 0:w], hT[:, cols(c)], ACT.Square).then_inc(csq.sem, 1)
                    c = s - 2
                    if 0 <= c < NC:
                        w = CH[c][1] * D
                        act.wait_ge(var_ps.sem, var_ps.at(l, c + 1))
                        f(cb[:, 1, c % 2, 0:w], ps[:, 4 + c % 2, 0:w], ACT.Ln,
                          bias=eps_ln[:, 0:1]).then_inc(ln_log.sem, 1)
                        act.wait_ge(ln_log.sem, ln_log.at(l, c + 1))
                        f(cb[:, 1, c % 2, 0:w], cb[:, 1, c % 2, 0:w], ACT.Exp,
                          scale=-0.5).then_inc(ln_sd.sem, 1)
                for s in range(NC + 2):
                    c = s
                    if c < NC:
                        act.wait_ge(scaled.sem, scaled.at(l, c + 1))
                        f(hT[:, cols(c)], hT[:, cols(c)], ACT.Identity, scale=v_sb[:, 3:4],
                          bias=v_sb[:, 4:5]).then_inc(affine.sem, 1)
                    c = s - 1
                    if 0 <= c < NC:
                        w = CH[c][1] * D
                        act.wait_ge(negpart.sem, negpart.at(l, c + 1))
                        f(cb[:, 0, c % 2, 0:w], cb[:, 0, c % 2, 0:w], ACT.Exp).then_inc(expd.sem, 1)
                    c = s - 2
                    if next_layer and 0 <= c < NC:
                        for t in range(CH[c][0], CH[c][0] + CH[c][1]):
                            project(l, t)

            with act.Fori(0, L - 1) as l:
                stage_a(l)
                stage_b(l, True)
            stage_a(L - 1)
            stage_b(L - 1, False)
            for c, (t0, nt) in enumerate(CH):
                act.wait_ge(f_var, c + 1)
                f(fsd[:, c % 2, 0:nt], fmv[:, c % 2, 0:nt, 1], ACT.Sqrt, bias=eps_ln[:, 0:1]).then_inc(f_sd, 1)

        @block.vector
        def _(dve):
            v = nc.vector
            ch = Chain(dve, s_dch)
            TT, TS, STT = v.tensor_tensor, v.tensor_scalar, v.scalar_tensor_tensor
            dve.wait_ge(s_dst, 16)
            ch.step(TS(digit_i[:, 0, :], dst_i[:, :], P - 1, None, ALU.bitwise_and))
            ch.step(TS(digit_i[:, 1, :], dst_i[:, :], 7, None, ALU.logical_shift_right))
            ch.wait()
            ch.step(v.tensor_copy(digit_b[:, :, :], digit_i[:, :, :]))
            ch.wait()
            dve.wait_ge(s_const, 3)

            def hots(b, at):
                lo = digit_b[:, 0:1, bass.ds(at, HC)]
                hi = digit_b[:, 1:2, bass.ds(at, HC)]
                TT(hot_lo[:, b, :, :], digits[0:EP, :, :], lo.to_broadcast([EP, P, HC]), ALU.is_equal)
                TT(hot_hi[:, b, :, :], digits[0:EP, 0:T, :], hi.to_broadcast([EP, T, HC]),
                   ALU.is_equal).then_inc(s_digits, 1)

            hots(0, 0)
            hots(1, HC)
            with dve.Fori(0, (HCH - 1) // 2 - 1) as i:
                dve.wait_ge(s_hist, 2 * i + 1)
                hots(0, (2 * HC) * i + 2 * HC)
                dve.wait_ge(s_hist, 2 * i + 2)
                hots(1, (2 * HC) * i + 3 * HC)
            dve.wait_ge(s_hist, HCH - 2)
            hots(0, (HCH - 1) * HC)
            dve.wait_ge(s_hist, HCH)
            v.tensor_copy(deg[:, :], ps[:, 0, 0:T]).then_inc(s_deg, 1)
            dve.wait_ge(s_deg, 1)
            ch.step(TS(small[:, 0, :], deg[:, :], -1.0, float(BINS - 1), ALU.mult, ALU.add))
            ch.wait()
            ch.step(TS(key_b[:, :], small[:, 0, :], 0.0, None, ALU.max))
            ch.wait()
            dve.wait_ge(s_pre, 1)
            ch.step(v.memset(small[:, 1, :], 1.0))
            ch.step(v.memset(place[:, 1, :], 1.0))
            ch.wait()
            ch.step(v.tensor_tensor_scan(small[:, 2, :], small[:, 1, :], ps[:, 1, 32:32 + T], 0.0, ALU.mult, ALU.add))
            ch.wait()
            ch.step(TT(small[:, 3, :], small[:, 2, :], ps[:, 1, 32:32 + T], ALU.subtract))
            ch.wait()
            ch.step(TT(start[:, :], small[:, 3, :], ps[:, 1, 0:T], ALU.add))
            ch.wait()
            TT(hot_bin[:, :, :], digits[:, 0:BINS, :],
               key_b[:, :].rearrange("p (a t) -> p a t", a=1).to_broadcast([P, BINS, T]),
               ALU.is_equal).then_inc(s_bins, 1)
            v.tensor_copy(info[:, :, 0], start[:, :])
            v.tensor_copy(info[:, :, 1], deg[:, :])
            v.tensor_copy(info[:, :, 2], node_no[:, :])
            ch.step(v.memset(info[:, :, 3], 0))
            dve.wait_ge(s_places, 1)
            for q in range(4):
                first = 0.0 if q == 0 else place[:, 0, q * BB * T - 1:q * BB * T]
                ch.step(v.tensor_tensor_scan(place[:, 0, q * BB * T:(q + 1) * BB * T],
                                             place[:, 1, q * BB * T:(q + 1) * BB * T],
                                             ps[:, 4 + q, 0:BB * T], first, ALU.mult, ALU.add))
                ch.wait()
            ch.step(TT(over_bins(place[:, 1, :]), over_bins(place[:, 0, :]), ps[:, 4:8, 0:BB * T], ALU.subtract))
            ch.wait()
            ch.step(TT(over_bins(place[:, 0, :]), over_bins(place[:, 1, :]), ps[:, 0:4, 0:BB * T], ALU.add))
            ch.wait()
            ch.step(TT(place[:, 1, :], place[:, 0, :], hot_bin[:, :, :].rearrange("p b t -> p (b t)"), ALU.mult))
            ch.wait()
            ch.step(v.tensor_reduce(small[:, 4, :], place[:, 1, :].rearrange("p (b t) -> p t b", t=T), AX.X, ALU.add))
            ch.wait()
            v.tensor_copy(rank_i[:, :], small[:, 4, :]).then_inc(s_info, 1)
            dve.wait_ge(s_infor, 16)
            ch.step(v.tensor_copy(node_i[:, :], info_r[:, :, 2]))
            ch.wait()
            TS(row_i[:, :], info_r[:, :, 0], 3, None, ALU.logical_shift_right).then_inc(s_rows, 1)
            v.tensor_copy(node_f[:, :], info_r[:, :, 2])
            v.tensor_copy(start_r[:, :], info_r[:, :, 0])
            v.tensor_copy(deg_r[:, :], info_r[:, :, 1]).then_inc(s_rows, 1)
            dve.wait_ge(s_rows, 2)
            for i in range(3):
                TS(bits_i[:, i, :], info_r[:, :, 0], 2 - i, 1, ALU.logical_shift_right, ALU.bitwise_and)
            ch.step(TS(small[:, 0, :], deg_r[:, :], 1.0, None, ALU.add))
            ch.wait()
            ch.step(v.tensor_copy(bits_f[:, :, :], bits_i[:, :, :]))
            ch.step(v.reciprocal(rdeg[:, :], small[:, 0, :]))

            def project(l, t):
                if t == 0:
                    dve.wait_ge(s_wc, 32 * (l + 2))
                dve.wait_ge(pqu_ps.sem, pqu_ps.at(l, t + 1))
                TT(pqu[:, t, 1:3, :].rearrange("p a d -> p (a d)"), ps[:, 6 + t % 2, 0:2 * D], b_qu_sb[:, :],
                   ALU.add).then_inc(qu_copied.sem, 1)

            for t in range(T):
                project(-1, t)
            dve.wait_ge(s_lnd, 1)
            ch.step(TS(amp[:, :], amp[:, :], 1.0 / DELTA, None, ALU.mult))
            ch.wait()
            ch.step(v.reciprocal(att[:, :], amp[:, :]))
            dve.wait_ge(s_wing, 16 * T)
            def win(b, w, o=0):
                return win_f[:, b, :].rearrange("p (t k) -> p t k", k=WL)[:, :, o:o + w]
            def per_node(ap, w):
                return ap.rearrange("p (t a) -> p t a", a=1).to_broadcast([P, T, w])
            ch.step(v.tensor_copy(win(0, WL), win_i[:, :, :]))
            w = WL
            for i, by in enumerate((4, 2, 1)):
                w -= by
                ch.wait()
                ch.step(TT(win(1, w), win(0, w, by), win(0, w), ALU.subtract))
                ch.wait()
                ch.step(TT(win(1, w), win(1, w), per_node(bits_f[:, i, :], w), ALU.mult))
                ch.wait()
                ch.step(TT(win(0, w), win(0, w), win(1, w), ALU.add))
            ch.step(TS(small[:, 1, :], deg_r[:, :], -1.0, None, ALU.add))
            ch.wait()
            wk = win(1, KW)
            wi = win_i[:, :, 0:KW].bitcast(FP32)
            ch.step(TT(wk, slot_no[:, :, :], per_node(small[:, 1, :], KW), ALU.is_equal))
            ch.step(TT(wi, win(0, KW), per_node(node_f[:, :], KW), ALU.is_equal))
            ch.wait()
            ch.step(TT(wk, wk, wi, ALU.mult))
            ch.wait()
            ch.step(v.tensor_reduce(small[:, 2, :], wk, AX.X, ALU.add))
            ch.wait()
            ch.step(TT(g_r[:, :], deg_r[:, :], small[:, 2, :], ALU.subtract))
            ch.wait()
            ch.step(TT(wk, slot_no[:, :, :], per_node(g_r[:, :], KW), ALU.is_lt))
            ch.step(TT(wi, win(0, KW), per_node(node_f[:, :], KW), ALU.subtract))
            ch.wait()
            ch.step(TT(wk, wk, wi, ALU.mult))
            ch.wait()
            ch.step(TT(index[:, :, :], wk, per_node(node_f[:, :], KW), ALU.add))
            ch.step(TT(small[:, 4, :], plan_sb[:, :], g_r[:, :], ALU.max))
            ch.wait()
            ch.step(TT(self_w[:, :], small[:, 0, :], small[:, 4, :], ALU.subtract))
            TT(small[:, 3, :], g_r[:, :], plan_sb[:, :], ALU.subtract).then_inc(s_idx, 1)
            dve.wait_ge(s_gT, 1)
            v.tensor_reduce(extra_t[:, :], ps[0:T, 4, 0:P], AX.X, ALU.max).then_inc(s_most, 1)
            dve.wait_ge(s_mostT, 1)
            ch.step(v.memset(small[0:1, 1, :], 1.0))
            ch.step(v.tensor_copy(extra_f[:, 0:T], ps[0:1, 5, 0:T]))
            ch.wait()
            ch.step(TS(extra_f[:, 0:T], extra_f[:, 0:T], 0.0, None, ALU.max))
            ch.wait()
            ch.step(v.tensor_reduce(extra_f[:, T:T + 1], extra_f[:, 0:T], AX.X, ALU.add))
            ch.step(v.tensor_tensor_scan(extra_f[:, T + 1:], small[0:1, 1, :], extra_f[:, 0:T], 0.0,
                                         ALU.mult, ALU.add))
            ch.wait()
            ch.step(TT(extra_f[:, T + 1:], extra_f[:, T + 1:], extra_f[:, 0:T], ALU.subtract))
            ch.wait()
            v.tensor_copy(extra_i[:, :], extra_f[:, :]).then_inc(s_extra, 1)
            dve.wait_ge(s_extra, 1)
            ch.restart()

            def groups(l, t):
                own = tile_groups[t]
                rest = GROUPS[own[1]][3] < GW
                for n in own:
                    j, w = GROUPS[n][1], GROUPS[n][3] * D
                    dve.wait_ge(gathered[n % R].sem, gathered[n % R].at(l, slot_before[n]))
                    if j <= rest:
                        continue
                    here = G[:, n % R, :]
                    if j == 1 + rest:
                        first, odd = G[:, own[0] % R, :], own[1]
                        for i, op in ((0, ALU.max), (1, ALU.min)):
                            ins = TT(acc[:, i, :], first, here, op)
                            if rest:
                                ch.step(ins)
                        if rest:
                            ch.wait()
                            w = GROUPS[odd][3] * D
                            for i, op in ((0, ALU.max), (1, ALU.min)):
                                ins = TT(acc[:, i, 0:w], acc[:, i, 0:w], G[:, odd % R, 0:w], op)
                        ins.then_inc(dve_used.sem, 2 + rest)
                        continue
                    dve.wait_ge(dve_used.sem, dve_used.at(l, n))
                    TT(acc[:, 0, :], acc[:, 0, :], here, ALU.max)
                    TT(acc[:, 1, :], acc[:, 1, :], here, ALU.min).then_inc(dve_used.sem, 1)

            def open_bases():
                own = pqu[:, :, 0, :]
                weight = self_w[:, :].rearrange("p (t a) -> p t a", a=1).to_broadcast([P, T, D])
                ch.step(v.tensor_copy(base_min, own))
                ch.step(TT(base_s1, own, weight, ALU.mult))
                ch.wait()
                ch.step(TT(base_s2, base_s1, own, ALU.mult))
                ch.wait()

            def extras(l):
                xc = Chain(dve, s_xch)
                valid, pos, new = ex_f[:, 0:1], ex_f[:, 1:2], ex_f[:, 2:3]

                def of_tile(ap, t):
                    return ap[:, bass.ds(t, 1)]

                def row(ap, t):
                    return ap[:, bass.ds(t, 1), :].rearrange("p a d -> p (a d)")

                total = dve.value_load(extra_i[0:1, T:T + 1], min_val=0, max_val=T * E)
                with dve.If(total > 0):
                    with dve.Fori(0, T) as t:
                        more = dve.value_load(extra_i[0:1, bass.ds(t, 1)], min_val=0, max_val=T * E)
                        ahead = dve.value_load(extra_i[0:1, bass.ds(t + (T + 1), 1)], min_val=0, max_val=T * E)
                        done = dve.snap(l * total + ahead)
                        xc.step(v.tensor_copy(ex_k[:, :], of_tile(plan_sb, t)))
                        xc.restart()
                        with dve.If(more > 0):
                            with dve.Fori(0, more) as j:
                                xc.step(TT(valid, ex_k[:, :], of_tile(g_r, t), ALU.is_lt))
                                xc.step(TT(pos, ex_k[:, :], of_tile(start_r, t), ALU.add))
                                xc.wait()
                                xc.step(TT(ex_arc[:, :], pos, valid, ALU.mult))
                                xc.wait()
                                dve.sem_inc(x_arc, 1)
                                dve.wait_ge(x_src, 16 * (done + j) + 16)
                                xc.step(TT(new, ex_src[:, :], of_tile(node_f, t), ALU.subtract))
                                xc.wait()
                                xc.step(TT(new, new, valid, ALU.mult))
                                xc.wait()
                                xc.step(TT(ex_node[:, :], new, of_tile(node_f, t), ALU.add))
                                xc.step(TS(ex_k[:, :], ex_k[:, :], 1.0, None, ALU.add))
                                xc.wait()
                                dve.sem_inc(x_node, 1)
                                dve.wait_ge(x_p, 16 * (done + j) + 16)
                                got = ex_p[:, 0, :]
                                top = pqu[:, bass.ds(t, 1), 0, :].rearrange("p a d -> p (a d)")
                                xc.step(TT(top, top, got, ALU.max))
                                xc.step(TT(row(base_min, t), row(base_min, t), got, ALU.min))
                                xc.step(TS(ex_p[:, 1, :], got, valid, None, ALU.mult))
                                xc.wait()
                                xc.step(TT(row(base_s1, t), row(base_s1, t), ex_p[:, 1, :], ALU.add))
                                xc.step(TT(ex_p[:, 2, :], ex_p[:, 1, :], got, ALU.mult))
                                xc.wait()
                                xc.step(TT(row(base_s2, t), row(base_s2, t), ex_p[:, 2, :], ALU.add))
                                xc.restart()
                        dve.nop()
                    dve.nop()
                dve.nop()

            def finals(l, t):
                A = agg[:, t % 2, :]
                own_q = pqu[:, t, 1, :]
                dve.wait_ge(dve_used.sem, dve_used.at(l, tile_groups[t][-1] + 1))
                if t >= 2:
                    dve.wait_ge(agg_turned.sem, agg_turned.at(l, t - 1))
                def four(ap):
                    return ap.rearrange("p (k d) -> p d k", k=GW)
                ch.step(v.tensor_reduce(tmp[:, 0, :], four(acc[:, 0, :]), AX.X, ALU.max))
                ch.step(v.tensor_reduce(tmp[:, 1, :], four(acc[:, 1, :]), AX.X, ALU.min))
                ch.wait()
                ch.step(TT(tmp[:, 0, :], tmp[:, 0, :], pqu[:, t, 0, :], ALU.max))
                ch.step(TT(tmp[:, 1, :], tmp[:, 1, :], base_min[:, t, :], ALU.min))
                ch.wait()
                ch.step(TT(A[:, 0:D], tmp[:, 0, :], own_q, ALU.add))
                ch.step(TT(A[:, D:2 * D], tmp[:, 1, :], own_q, ALU.add))
                dve.wait_ge(pe_used.sem, pe_used.at(l, tile_groups[t][-1] + 1))
                ch.step(v.tensor_reduce(tmp[:, 2, :], four(ps[:, t % 2, :]), AX.X, ALU.add))
                v.tensor_reduce(tmp[:, 3, :], four(ps[:, 2 + t % 2, :]), AX.X, ALU.add).then_inc(sums_read.sem, 1)
                dve.wait_ge(sums_read.sem, sums_read.at(l, t + 1))
                ch.step(TT(tmp[:, 2, :], tmp[:, 2, :], base_s1[:, t, :], ALU.add))
                ch.step(TT(tmp[:, 3, :], tmp[:, 3, :], base_s2[:, t, :], ALU.add))
                ch.wait()
                ch.step(TS(tmp[:, 2, :], tmp[:, 2, :], rdeg[:, t:t + 1], None, ALU.mult))
                ch.wait()
                ch.step(TT(tmp[:, 5, :], tmp[:, 2, :], tmp[:, 2, :], ALU.mult))
                ch.wait()
                ch.step(STT(tmp[:, 3, :], tmp[:, 3, :], rdeg[:, t:t + 1], tmp[:, 5, :], ALU.mult, ALU.subtract))
                ch.wait()
                TS(A[:, 3 * D:4 * D], tmp[:, 3, :], 0.0, None, ALU.max).then_inc(var_ready.sem, 1)

            def combine(l, t):
                U = u_sb[:, t % 2, :]
                dve.wait_ge(z_done.sem, z_done.at(l, t + 1))
                if t >= 2:
                    dve.wait_ge(u_turned.sem, u_turned.at(l, t - 1))
                ch.step(TT(U, ps[:, 6, 0:D], pqu[:, t, 2, :], ALU.add))
                ch.wait()
                ch.step(STT(U, ps[:, 6, D:2 * D], amp[:, t:t + 1], U, ALU.mult, ALU.add))
                ch.wait()
                STT(U, ps[:, 6, 2 * D:3 * D], att[:, t:t + 1], U, ALU.mult, ALU.add).then_inc(u_ready.sem, 1)

            def stage_a(l):
                dve.wait_ge(p_scattered.sem, p_scattered.at(l, 0))
                open_bases()
                extras(l)
                for s in range(T + 4):
                    if s < T:
                        groups(l, s)
                        finals(l, s)
                    if 0 <= s - 2 < T:
                        combine(l, s - 2)
                    t = s - 4
                    if 0 <= t < T:
                        dve.wait_ge(u_copied.sem, u_copied.at(l, t + 1))
                        n = P if t < T - 1 else LAST
                        ch.step(v.bn_stats(bstats[:, t, :], uT[:, t * P:t * P + n]))
                ch.wait()
                ch.step(v.bn_aggr(mv[:, 0:2], bstats[:, :, :].rearrange("p t s -> p (t s)")))
                ch.wait()
                TS(mv[:, 2:3], mv[:, 1:2], INV_N, BN_EPS, ALU.mult, ALU.add).then_inc(bn_var.sem, 1)
                dve.wait_ge(s_wa, 48 * (l + 1))
                dve.wait_ge(bn_sd.sem, bn_sd.at(l, 1))
                ch.step(v.reciprocal(mv[:, 5:6], mv[:, 3:4]))
                ch.wait()
                ch.step(STT(mv[:, 4:5], mv[:, 5:6], math.sqrt(INV_N), v_sb[:, 0:1], ALU.mult, ALU.mult))
                ch.wait()
                ch.step(TT(mv[:, 7:8], mv[:, 0:1], mv[:, 4:5], ALU.mult))
                ch.wait()
                TT(mv[:, 6:7], v_sb[:, 1:2], mv[:, 7:8], ALU.subtract).then_inc(bn_ready.sem, 1)

            def stage_b(l, next_layer):
                for s in range(NC + 2):
                    c = s
                    if c < NC:
                        w = CH[c][1] * D
                        t_c = cb[:, 0, c % 2, 0:w]
                        dve.wait_ge(biased.sem, biased.at(l, c + 1))
                        ch.step(STT(t_c, t_c, SLOPE, t_c, ALU.mult, ALU.max))
                        ch.wait()
                        TT(hT[:, cols(c)], hT[:, cols(c)], t_c, ALU.add).then_inc(resid.sem, 1)
                    c = s - 1
                    if 0 <= c < NC:
                        w = CH[c][1] * D
                        dve.wait_ge(mean_ps.sem, mean_ps.at(l, c + 1))
                        TT(hT[:, cols(c)], hT[:, cols(c)], ps[:, 2 + c % 2, 0:w], ALU.subtract)\
                            .then_inc(centred.sem, 1)
                    c = s - 2
                    if 0 <= c < NC:
                        w = CH[c][1] * D
                        sd = cb[:, 1, c % 2, 0:w]
                        dve.wait_ge(ln_sd.sem, ln_sd.at(l, c + 1))
                        TT(hT[:, cols(c)], hT[:, cols(c)], sd, ALU.mult).then_inc(scaled.sem, 1)
                for s in range(NC + 2):
                    c = s
                    if c < NC:
                        w = CH[c][1] * D
                        dve.wait_ge(affine.sem, affine.at(l, c + 1))
                        TS(cb[:, 0, c % 2, 0:w], hT[:, cols(c)], 0.0, None, ALU.min).then_inc(negpart.sem, 1)
                    c = s - 1
                    if 0 <= c < NC:
                        w = CH[c][1] * D
                        dve.wait_ge(expd.sem, expd.at(l, c + 1))
                        ch.step(STT(hT[:, cols(c)], hT[:, cols(c)], 0.0, cb[:, 0, c % 2, 0:w], ALU.max, ALU.add))
                        ch.wait()
                        TS(hT[:, cols(c)], hT[:, cols(c)], -1.0, None, ALU.add).then_inc(h_ready.sem, 1)
                    c = s - 2
                    if next_layer and 0 <= c < NC:
                        for t in range(CH[c][0], CH[c][0] + CH[c][1]):
                            project(l, t)

            with dve.Fori(0, L - 1) as l:
                stage_a(l)
                stage_b(l, True)
                ch.restart()
            stage_a(L - 1)
            stage_b(L - 1, False)
            for c, (t0, nt) in enumerate(CH):
                w = nt * D
                dve.wait_ge(f_turned, c + 1)
                TT(y_sb[:, c % 2, 0:w], ps[:, 6 + c % 2, 0:w],
                   x_r[:, t0:t0 + nt, :].rearrange("p t d -> p (t d)"), ALU.add).then_inc(f_added, 1)
                dve.wait_ge(f_added, c + 1)
                for i in range(nt):
                    ch.step(v.bn_stats(fstats[:, i, :], y_sb[:, c % 2, i * D:(i + 1) * D]))
                ch.wait()
                for i in range(nt):
                    ins = v.bn_aggr(fmv[:, c % 2, i, :], fstats[:, i, :])
                ins.then_inc(f_var, 1)
                dve.wait_ge(f_var, c + 1)
                dve.wait_ge(f_sd, c + 1)
                ch.step(v.reciprocal(fsd[:, c % 2, 0:nt], fsd[:, c % 2, 0:nt]))
                ch.wait()
                if c >= 2:
                    dve.wait_ge(f_out[c % 2], rows_out(c - 2))
                for i in range(nt):
                    TS(o_sb[:, c % 2, i * D:(i + 1) * D], y_sb[:, c % 2, i * D:(i + 1) * D],
                       fmv[:, c % 2, i, 0:1], fsd[:, c % 2, i:i + 1], ALU.subtract, ALU.mult).then_inc(f_done, 1)


def kernel(x, src, dst, L0_gnn_Mw, L0_gnn_Mb, L0_gnn_Uw, L0_gnn_Ub, L0_gnn_bn_g, L0_gnn_bn_b,
           L0_gnn_mix_w, L0_gnn_mix_b, L0_gnn_ln_g, L0_gnn_ln_b):
    import numpy as np
    import concourse.bacc as bacc
    from concourse.bass_utils import run_bass_kernel_spmd

    Mw, Uw, mix = (np.asarray(a) for a in (L0_gnn_Mw, L0_gnn_Uw, L0_gnn_mix_w))
    L, D = Mw.shape[0], Mw.shape[1]
    w_pqu = np.concatenate([Mw[:, :, :D], Mw[:, :, D:], Uw[:, :, :D]], axis=1).transpose(0, 2, 1)
    b_qu = np.concatenate([np.asarray(L0_gnn_Mb), np.asarray(L0_gnn_Ub)], axis=1)
    w_u = Uw[:, :, D:].reshape(L, D, 3, 4, D).transpose(0, 4, 3, 2, 1).reshape(L, D, 4, 3 * D)
    v_cols = np.stack([np.asarray(a) for a in (L0_gnn_bn_g, L0_gnn_bn_b, L0_gnn_mix_b, L0_gnn_ln_g,
                                               L0_gnn_ln_b)], axis=2)
    arrays = {"x": np.asarray(x), "src": np.asarray(src), "dst": np.asarray(dst), "w_pqu": w_pqu, "b_qu": b_qu,
              "w_u": w_u, "w_mix": mix.transpose(0, 2, 1), "v_cols": v_cols}
    arrays = {k: np.ascontiguousarray(a) for k, a in arrays.items()}
    nc = bacc.Bacc("TRN2", target_bir_lowering=False, num_devices=1)
    args = [nc.dram_tensor(f"in_{k}", a.shape, mybir.dt.from_np(a.dtype), kind="ExternalInput").ap()
            for k, a in arrays.items()]
    out = nc.dram_tensor("out_h", arrays["x"].shape, FP32, kind="ExternalOutput").ap()
    build(nc, *args, out)
    r = run_bass_kernel_spmd(nc, [{f"in_{k}": a for k, a in arrays.items()}], core_ids=[0])
    return r.results[0]["out_h"]
```
